# Optimizing a Trainium2 kernel written in Bass

```python
import numpy as np
import jax
import jax.numpy as jnp

def _softmax(x, axis=-1):
    return jax.nn.softmax(x, axis=axis)

def _gelu(x):
    return jax.nn.gelu(x, approximate=True)

def _silu(x):
    return jax.nn.silu(x)

def _sigmoid(x):
    return jax.nn.sigmoid(x)

def _layernorm(x, axis=-1, eps=1e-05):
    m = jnp.mean(x, axis=axis, keepdims=True)
    v = jnp.var(x, axis=axis, keepdims=True)
    return (x - m) / jnp.sqrt(v + eps)

def _scatter_add(tgt, idx, src, axis=0):
    return tgt.at[idx].add(src)

def _segment_sum(src, seg, n):
    return jax.ops.segment_sum(src, seg, n)
kernel_name = 'mk_seq_postln_d1_jaxref_r8_d03870'

def setup_inputs(seed: int=0):
    np.random.seed(seed)
    _w = jnp.asarray

    def _L0_attn_setup():
        import jax, jax.numpy as jnp
        import numpy as np
        import math
        D_MODEL = 128
        NUM_HEADS = 16
        HEAD = D_MODEL // NUM_HEADS
        EPS = 1e-05

        def _layernorm(x, w, b):
            mean = jnp.mean(x, axis=-1, keepdims=True)
            var = jnp.var(x, axis=-1, keepdims=True)
            return (x - mean) * w / jnp.sqrt(var + EPS) + b
        key = jax.random.key(seed)
        ks = jax.random.split(key, 5)
        x = jax.random.normal(ks[0], (2, 256, D_MODEL), dtype=jnp.float32)
        wq = jax.random.uniform(ks[1], (NUM_HEADS, D_MODEL, HEAD), dtype=jnp.float32) * 0.02
        wk = jax.random.uniform(ks[2], (NUM_HEADS, D_MODEL, HEAD), dtype=jnp.float32) * 0.02
        wv = jax.random.uniform(ks[3], (NUM_HEADS, D_MODEL, HEAD), dtype=jnp.float32) * 0.02
        wo = jax.random.uniform(ks[4], (D_MODEL, D_MODEL), dtype=jnp.float32) * 0.02
        ln_w = jnp.ones((D_MODEL,), dtype=jnp.float32)
        ln_b = jnp.zeros((D_MODEL,), dtype=jnp.float32)
        return {'x': x, 'ln_w': ln_w, 'ln_b': ln_b, 'wq': wq, 'wk': wk, 'wv': wv, 'wo': wo}
    _L0_attn_in = _L0_attn_setup()

    def _L0_ffn_setup():
        import jax, jax.numpy as jnp
        import numpy as np
        ALPHA = 1.0
        key = jax.random.key(seed)
        ks = jax.random.split(key, 7)
        B, S, IN, OUT = (8, 1024, 128, 128)
        RANK, DDIM, UDIM = (4, 100, 50)
        return {'hidden_states': jax.random.normal(ks[0], (B, S, IN), dtype=jnp.float32), 'W': jax.random.normal(ks[1], (OUT, IN), dtype=jnp.float32) * 0.02, 'b': jax.random.normal(ks[2], (OUT,), dtype=jnp.float32) * 0.02, 'lora_down': jax.random.normal(ks[3], (RANK, DDIM), dtype=jnp.float32) * 0.1, 'lora_up': jax.random.normal(ks[4], (UDIM, RANK), dtype=jnp.float32) * 0.1, 'down_aux': jax.random.normal(ks[5], (DDIM, IN), dtype=jnp.float32) * 0.03, 'up_aux': jax.random.normal(ks[6], (OUT, UDIM), dtype=jnp.float32) * 0.03}
    _L0_ffn_in = _L0_ffn_setup()
    _d = {'L0_attn_x': _L0_attn_in['x'], 'L0_attn_ln_w': _L0_attn_in['ln_w'], 'L0_attn_ln_b': _L0_attn_in['ln_b'], 'L0_attn_wq': _L0_attn_in['wq'], 'L0_attn_wk': _L0_attn_in['wk'], 'L0_attn_wv': _L0_attn_in['wv'], 'L0_attn_wo': _L0_attn_in['wo'], 'L0_ffn_W': _L0_ffn_in['W'], 'L0_ffn_b': _L0_ffn_in['b'], 'L0_ffn_lora_down': _L0_ffn_in['lora_down'], 'L0_ffn_lora_up': _L0_ffn_in['lora_up'], 'L0_ffn_down_aux': _L0_ffn_in['down_aux'], 'L0_ffn_up_aux': _L0_ffn_in['up_aux']}
    _x0 = _d['L0_attn_x']
    _d['L0_attn_x'] = jax.random.normal(jax.random.fold_in(jax.random.key(seed), 1), (32, 256, 128), dtype=_x0.dtype)
    del _x0
    return _d

def reference(L0_attn_x, L0_attn_ln_w, L0_attn_ln_b, L0_attn_wq, L0_attn_wk, L0_attn_wv, L0_attn_wo, L0_ffn_W, L0_ffn_b, L0_ffn_lora_down, L0_ffn_lora_up, L0_ffn_down_aux, L0_ffn_up_aux):

    def _L0_attn_ref(x, ln_w, ln_b, wq, wk, wv, wo):
        import jax, jax.numpy as jnp
        import numpy as np
        import math
        D_MODEL = 128
        NUM_HEADS = 16
        HEAD = D_MODEL // NUM_HEADS
        EPS = 1e-05

        def _layernorm(x, w, b):
            mean = jnp.mean(x, axis=-1, keepdims=True)
            var = jnp.var(x, axis=-1, keepdims=True)
            return (x - mean) * w / jnp.sqrt(var + EPS) + b
        y = _layernorm(x, ln_w, ln_b)
        seq_len = y.shape[-2]
        q = jnp.einsum('bsd,hde->bhse', y, wq)
        k = jnp.einsum('bsd,hde->bhse', y, wk)
        v = jnp.einsum('bsd,hde->bhse', y, wv)
        scores = jnp.einsum('bhse,bhte->bhst', q, k) / math.sqrt(HEAD)
        causal = jnp.triu(jnp.full((seq_len, seq_len), -jnp.inf, dtype=scores.dtype), k=1)
        scores = scores + causal
        weights = jax.nn.softmax(scores, axis=-1)
        attn = jnp.einsum('bhst,bhte->bshe', weights, v)
        attn = attn.reshape(*attn.shape[:-2], -1)
        out = attn @ wo
        return out + x

    def _L0_ffn_ref(hidden_states, W, b, lora_down, lora_up, down_aux, up_aux):
        import jax, jax.numpy as jnp
        import numpy as np
        ALPHA = 1.0
        lilora_weight = up_aux @ (lora_up @ (lora_down @ down_aux))
        base = jnp.einsum('bsi,oi->bso', hidden_states, W) + b
        delta = jnp.einsum('bsi,oi->bso', hidden_states, lilora_weight)
        return base + ALPHA * delta
    x = L0_attn_x
    x = _layernorm(x + _L0_attn_ref(x, L0_attn_ln_w, L0_attn_ln_b, L0_attn_wq, L0_attn_wk, L0_attn_wv, L0_attn_wo), axis=-1)
    x = _layernorm(x + _L0_ffn_ref(x, L0_ffn_W, L0_ffn_b, L0_ffn_lora_down, L0_ffn_lora_up, L0_ffn_down_aux, L0_ffn_up_aux), axis=-1)
    return x

_drawn_inputs = setup_inputs


def setup_inputs(seed=0):
    import zlib

    import numpy as np

    out = dict(_drawn_inputs(seed))
    spreads = {'L0_attn_ln_w': (1.0, 0.6), 'L0_attn_ln_b': (0.0, 0.8)}
    factors = {'L0_attn_wq': 8.0,
     'L0_attn_wk': 8.0,
     'L0_attn_wv': 8.0,
     'L0_attn_wo': 8.0,
     'L0_ffn_b': 8.553,
     'L0_ffn_lora_down': 3.965,
     'L0_ffn_lora_up': 4.372,
     'L0_ffn_down_aux': 3.672,
     'L0_ffn_up_aux': 4.074}
    for name, (base, spread) in spreads.items():
        noise = np.random.default_rng([zlib.crc32(name.encode()), seed]).standard_normal(out[name].shape)
        drawn = base * np.exp(spread * noise) if base else spread * noise
        out[name] = jnp.asarray(drawn.astype(out[name].dtype))
    for name, factor in factors.items():
        out[name] = (out[name] * factor).astype(out[name].dtype)
    return out
```

```python
from contextlib import ExitStack

import concourse.bass as bass
from concourse import mybir

F32 = mybir.dt.float32
BF16 = mybir.dt.bfloat16
ALU = mybir.AluOpType
ACT = mybir.ActivationFunctionType

P = 128
BATCHES, SEQ, D = 32, 256, 128
HEADS = 16
HD = D // HEADS
NB = SEQ // P
PARTS = 3
PART_ROWS = PARTS * HD
SPLIT_ROWS = PARTS * PART_ROWS
MAX_PARTS = 2
SCORE_ROWS = SPLIT_ROWS + MAX_PARTS
GROUP = 4
GROUPS = HEADS // GROUP
HALF = HEADS // 2
VW = P // GROUP
PW = SEQ + P
EPS = 1e-5
SCALE = float(HD) ** -0.5
LOWEST = -3.0e38
RING = 3
FIRST, LAST = -3, BATCHES + 2
LOOP_FROM = 4
LOOP_TO = LOOP_FROM + (BATCHES - 4 - LOOP_FROM) // RING * RING
RANK, DDIM, UDIM = 4, 100, 50


class Iteration:

    def __init__(self, eng, base, u, cache):
        self.eng, self.base, self.u, self.cache = eng, base, u, cache
        self.static = isinstance(base, int)

    def runs(self, offset):
        return not self.static or 0 <= self.base + self.u + offset < BATCHES

    def batch(self, offset):
        return self.base + (self.u + offset)

    def ring(self, offset):
        return ((self.base if self.static else LOOP_FROM) + self.u + offset) % RING

    def done(self, offset, per=1):
        c = self.u + offset + 1
        if self.static:
            return max(0, per * (self.base + c))
        if (c, per) not in self.cache:
            self.cache[c, per] = self.eng.snap((self.base + c) * per if per > 1 else self.base + c)
        return self.cache[c, per]


def iterate(eng, step):
    for it in range(FIRST, LOOP_FROM):
        step(Iteration(eng, it, 0, {}))
    with eng.Fori(LOOP_FROM, LOOP_TO - RING + 1, RING) as base:
        cache = {}
        for u in range(RING):
            step(Iteration(eng, base, u, cache))
    for it in range(LOOP_TO, LAST + 1):
        step(Iteration(eng, it, 0, {}))


def build(nc, x, ln_w, ln_b, wq, wk, wv, wo, w_t, bias, down_t, up_t, down_aux, up_aux_t, out):
    with ExitStack() as ctx:
        def sb(name, shape, dt=F32):
            return ctx.enter_context(nc.sbuf_tensor(name, shape, dt))

        def sem(name):
            return ctx.enter_context(nc.semaphore(name))

        def sems(name, n):
            return [sem(f"{name}{i}") for i in range(n)]

        max_bank = [ctx.enter_context(nc.psum_tensor(f"max_bank{i}", [P, 512], F32)) for i in range(2)]
        score_bank = [ctx.enter_context(nc.psum_tensor(f"score_bank{i}", [P, 512], F32)) for i in range(2)]
        pv_bank = [ctx.enter_context(nc.psum_tensor(f"pv_bank{i}", [P, 512], F32)) for i in range(2)]
        bank6 = ctx.enter_context(nc.psum_tensor("bank6", [P, 512], F32))
        bank7 = ctx.enter_context(nc.psum_tensor("bank7", [P, 512], F32))

        ident = sb("ident", [P, P])
        ident_b = sb("ident_b", [P, P], BF16)
        causal = sb("causal", [P, SEQ])
        ones_row = sb("ones_row", [1, P])
        wq_s, wk_s, wv_s, wo_s = (sb(n, [P, D]) for n in ("wq_s", "wk_s", "wv_s", "wo_s"))
        wf_s = sb("wf_s", [P, D])
        w_raw = sb("w_raw", [P, D])
        lnw_s, lnb_s = sb("lnw_s", [P, 1]), sb("lnb_s", [P, 1])
        bias_row = sb("bias_row", [1, D])
        bias_s = sb("bias_s", [P, D])
        down_s, up_s = sb("down_s", [DDIM, RANK]), sb("up_s", [RANK, UDIM])
        daux_s, uaux_s = sb("daux_s", [DDIM, D]), sb("uaux_s", [UDIM, D])
        low1, low2 = sb("low1", [RANK, D]), sb("low2", [UDIM, D])

        zero_rows = sb("zero_rows", [MAX_PARTS * HEADS, SEQ], BF16)
        xa = sb("xa", [P, NB, D])
        power = sb("power", [P, NB])
        st1, mv1, ve1, rs1 = sb("st1", [P, NB, 6]), sb("mv1", [P, NB, 2]), sb("ve1", [P, NB]), sb("rs1", [P, NB])
        xhat = sb("xhat", [P, NB, D])
        yT = sb("yT", [P, SEQ])
        parts = sb("parts", [P, PARTS, 2, SEQ], BF16)
        rest = sb("rest", [P, 2, SEQ])
        v_ext = [sb(f"v_ext{i}", [P, NB, HEADS, VW]) for i in range(RING)]
        qx = [sb(f"qx{i}", [P, HEADS, SEQ], BF16) for i in range(RING)]
        kx = [sb(f"kx{i}", [P, HEADS, SEQ], BF16) for i in range(RING)]
        rowmax = [sb(f"rowmax{i}", [P, NB, HALF]) for i in range(2)]
        mpart = [sb(f"mpart{i}", [P, NB, MAX_PARTS, HALF], BF16) for i in range(2)]
        mT = [sb(f"mT{i}", [MAX_PARTS * HALF, SEQ], BF16) for i in range(2)]
        probs = sb("probs", [P, HEADS, 2 * SEQ])
        pv_s = [sb(f"pv_s{i}", [P, SEQ]) for i in range(2)]
        rden = sb("rden", [P, NB, GROUP])
        attn = sb("attn", [P, NB, D])
        attnT = sb("attnT", [P, SEQ])
        xr = sb("xr", [P, NB, D])
        z = sb("z", [P, NB, D])
        st2, mv2, ve2, rs2 = sb("st2", [P, NB, 6]), sb("mv2", [P, NB, 2]), sb("ve2", [P, NB]), sb("rs2", [P, NB])
        nm2 = sb("nm2", [P, NB])
        x1 = sb("x1", [P, NB, D])
        x1b = sb("x1b", [P, NB, D])
        x1T = sb("x1T", [P, SEQ])
        f = sb("f", [P, NB, D])
        st3, mv3, ve3, rs3 = sb("st3", [P, NB, 6]), sb("mv3", [P, NB, 2]), sb("ve3", [P, NB]), sb("rs3", [P, NB])
        y = sb("y", [P, NB, D])

        q_rows = nc.dram_tensor("q_rows", [(PART_ROWS + MAX_PARTS) * HEADS, SEQ], BF16).ap()
        k_rows = nc.dram_tensor("k_rows", [(2 * PARTS - 1) * P, SEQ], BF16).ap()

        s_w = sem("weights_loaded")
        s_const = sem("constants_made")
        s_zero = sem("zero_rows_made_and_stored")
        s_const2 = sem("buffers_filled")
        s_low = sem("low_rank_product")
        s_lowc = sem("low_rank_copied")
        s_xa, s_xr, s_st = sem("xa_loaded"), sem("xr_loaded"), sem("y_stored")
        s_ve1, s_ve2, s_ve3 = (sem(f"variance_plus_eps{i}") for i in (1, 2, 3))
        s_stat1, s_mv1, s_rs1, s_xhat = sem("stats1"), sem("mean_var1"), sem("rstd1"), sem("xhat_ready")
        s_xT, s_yT = sem("xT_in_bank6"), sem("yT_ready")
        s_qk, s_p1, s_rest, s_p2, s_p3 = (sem("qk_in_bank6"), sem("parts1_ready"), sem("rest_ready"),
                                          sem("parts2_ready"), sem("parts3_ready"))
        s_stored = sem("parts_stored")
        s_expand = sem("heads_expanded")
        s_v, s_vx = sem("v_in_bank6"), sem("v_ext_ready")
        s_mscore, s_mread = sems("max_scores_in_bank_h", HEADS), sems("row_max_of_h", HEADS)
        s_mp1, s_mp2 = sems("max_part1_", 2), sems("max_part2_", 2)
        s_mTp, s_mT = sems("maxT_in_bank", 2), sems("maxT_ready", 2)
        s_mrow = sems("max_rows_loaded", 2)
        s_score, s_exp = sems("scores_in_bank_h", HEADS), sems("exp_of_h", HEADS)
        s_mask = sems("probs_masked_group", GROUPS)
        s_pv, s_pvs = sems("pv_in_bank_group", GROUPS), sems("pv_copied_group", GROUPS)
        s_ot, s_rden, s_norm = sems("pvT_in_bank7_group", GROUPS), sems("rden_group", GROUPS), sems("attn_group", GROUPS)
        s_aT, s_aTs = sem("attnT_in_bank7"), sem("attnT_ready")
        s_wo, s_z = sem("out_in_bank7"), sem("z_ready")
        s_stat2, s_mv2, s_rs2, s_nm2, s_x1 = sem("stats2"), sem("mean_var2"), sem("rstd2"), sem("shift2"), sem("x1_ready")
        s_x1b, s_x1T, s_x1Ts = sem("x1_plus_bias"), sem("x1T_in_bank6"), sem("x1T_ready")
        s_ff, s_f = sem("linear_in_bank6"), sem("f_ready")
        s_stat3, s_mv3, s_rs3, s_y = sem("stats3"), sem("mean_var3"), sem("rstd3"), sem("y_ready")

        weights = [(wq_s, wq), (wk_s, wk), (wv_s, wv), (wo_s, wo), (w_raw, w_t), (lnw_s, ln_w), (lnb_s, ln_b),
                   (bias_row, bias), (down_s, down_t), (up_s, up_t), (daux_s, down_aux), (uaux_s, up_aux_t)]
        N_W = 16 * len(weights)
        N_CONST = 7
        EXPAND = 16 * 2 * PARTS
        STORES = 16 * 3
        MAX_ROWS = 16 * MAX_PARTS

        s_passed = {e: sem(f"waits_passed_{e}") for e in ("sp", "pool", "dve")}

        def alone(eng, name):
            eng.sem_inc(s_passed[name], 1)

        block = ctx.enter_context(nc.Block())

        def rows(dram, batch):
            return dram[bass.ds(batch, 1), :, :].rearrange("o (n p) d -> p (o n) d", p=P)

        @block.sync
        def _(sp):
            sp.dma_start(xa[:, :, :], rows(x, 0)).then_inc(s_xa, 16)
            for tile, dram in weights:
                sp.dma_start(tile[:, :], dram[:, :]).then_inc(s_w, 16)
            sp.wait_ge(s_zero, 1)
            sp.dma_start(q_rows[PARTS * P:, :], zero_rows[:, :]).then_inc(s_zero, 16)
            sp.wait_ge(s_zero, 17)
            sp.wait_ge(s_const2, 2)

            def store_parts(it):
                for dram, which, first, n in ((q_rows, 0, 0, PARTS), (k_rows, 1, 0, PARTS), (k_rows, 1, PARTS, PARTS - 1)):
                    sp.dma_start(dram[first * P:(first + n) * P, :].rearrange("(i p) s -> p i s", p=P),
                                 parts[:, 0:n, which, :]).then_inc(s_stored, 16)

            def expand(it):
                r = it.ring(2)
                q, k = (t.rearrange("(r h) s -> r h s", h=HEADS) for t in (q_rows, k_rows))
                for turn in range(PARTS):
                    a, n = turn * PART_ROWS, PART_ROWS + (MAX_PARTS if turn == PARTS - 1 else 0)
                    sp.dma_start(qx[r][a:a + n, :, :], q[0:n, :, :]).then_inc(s_expand, 16)
                    sp.dma_start(kx[r][a:a + PART_ROWS, :, :],
                                 k[turn * HD:turn * HD + PART_ROWS, :, :]).then_inc(s_expand, 16)

            def max_rows(it, half, offset):
                sp.wait_ge(s_mT[half], it.done(offset))
                for part in range(MAX_PARTS):
                    sp.dma_start(qx[it.ring(offset)][SPLIT_ROWS + part:SPLIT_ROWS + part + 1,
                                                     half * HALF:(half + 1) * HALF, :],
                                 mT[half][part * HALF:(part + 1) * HALF, :]).then_inc(s_mrow[half], 16)

            def step(it):
                if it.runs(0):
                    max_rows(it, 1, 0)
                if it.runs(-3):
                    sp.wait_ge(s_y, it.done(-3))
                    sp.dma_start(rows(out, it.batch(-3)), y[:, :, :]).then_inc(s_st, 16)
                if it.runs(2):
                    sp.wait_ge(s_expand, it.done(1, EXPAND))
                    alone(sp, "sp")
                    sp.wait_ge(s_p3, it.done(2))
                    store_parts(it)
                    sp.wait_ge(s_score[HEADS - 1], it.done(-1))
                    alone(sp, "sp")
                    sp.wait_ge(s_stored, it.done(2, STORES))
                    expand(it)
                if it.runs(1):
                    max_rows(it, 0, 1)
                if it.runs(4):
                    sp.wait_ge(s_xhat, it.done(3))
                    sp.dma_start(xa[:, :, :], rows(x, it.batch(4))).then_inc(s_xa, 16)
                if it.runs(0):
                    sp.wait_ge(s_z, it.done(-1))
                    sp.dma_start(xr[:, :, :], rows(x, it.batch(0))).then_inc(s_xr, 16)

            iterate(sp, step)
            sp.wait_ge(s_st, 16 * BATCHES)

        @block.gpsimd
        def _(pool):
            for t in kx:
                ins = pool.memset(t[:, :, :], -1.0)
            ins.then_inc(s_const2, 1)
            pool.memset(ident[:, :], 0.0).then_inc(s_const, 1)
            pool.memset(ident_b[:, :], 0.0).then_inc(s_const, 1)
            pool.memset(causal[:, :], 0.0).then_inc(s_const, 1)
            pool.memset(power[:, :], -0.5).then_inc(s_const, 1)
            pool.wait_ge(s_const, 4)
            for m in (ident, ident_b):
                pool.affine_select(out=m[:, :], in_=m[:, :], compare_op=ALU.not_equal, fill=1.0,
                                   base=0, pattern=[[-1, P]], channel_multiplier=1).then_inc(s_const, 1)
            pool.affine_select(out=causal[:, P:SEQ], in_=causal[:, P:SEQ], compare_op=ALU.is_ge, fill=LOWEST,
                               base=0, pattern=[[-1, P]], channel_multiplier=1).then_inc(s_const, 1)

            def split_max(it, half, offset):
                pool.wait_ge(s_mread[half * HALF + HALF - 1], it.done(offset))
                pool.wait_ge(s_mTp[half], it.done(offset - 1))
                alone(pool, "pool")
                pool.tensor_copy(mpart[half][:, :, 0, :], rowmax[half][:, :, :]).then_inc(s_mp1[half], 1)
                pool.wait_ge(s_mp1[half], it.done(offset))
                pool.tensor_tensor(mpart[half][:, :, 1, :], rowmax[half][:, :, :], mpart[half][:, :, 0, :],
                                   ALU.subtract).then_inc(s_mp2[half], 1)

            def mask(it, group, offset):
                for h in range(GROUP * group, GROUP * group + GROUP):
                    pool.wait_ge(s_exp[h], it.done(offset))
                alone(pool, "pool")
                t = probs[:, GROUP * group:GROUP * group + GROUP, :].rearrange("p h (c s) -> p (h c) s", s=SEQ)[:, :, 0:P]
                pool.affine_select(out=t, in_=t, compare_op=ALU.is_ge, fill=0.0, base=0,
                                   pattern=[[0, GROUP * NB], [1, P]], channel_multiplier=-1)\
                    .then_inc(s_mask[group], 1)

            def rstd(it, ve, rs, added, signal, offset):
                pool.wait_ge(added, it.done(offset))
                pool.tensor_tensor(rs[:, :], ve[:, :], power[:, :], ALU.pow).then_inc(signal, 1)

            def normalise(it, source, stats, scale, target, ready, offset):
                for n in range(NB):
                    ins = pool.tensor_scalar(target[:, n, :], source[:, n, :], stats[:, n, 0:1], scale[:, n:n + 1],
                                             ALU.subtract, ALU.mult)
                ins.then_inc(ready, 1)

            def step(it):
                if it.runs(0):
                    split_max(it, 1, 0)
                if it.runs(-1):
                    mask(it, GROUPS - 1, -1)
                if it.runs(-2):
                    rstd(it, ve2, rs2, s_ve2, s_rs2, -2)
                if it.runs(-3):
                    rstd(it, ve3, rs3, s_ve3, s_rs3, -3)
                    pool.wait_ge(s_rs3, it.done(-3))
                    pool.wait_ge(s_st, it.done(-4, 16))
                    alone(pool, "pool")
                    normalise(it, f, mv3, rs3, y, s_y, -3)
                if it.runs(0):
                    mask(it, 0, 0)
                if it.runs(2):
                    pool.wait_ge(s_p2, it.done(2))
                    pool.tensor_tensor(parts[:, 2, :, :], rest[:, :, :], parts[:, 1, :, :],
                                       ALU.subtract).then_inc(s_p3, 1)
                if it.runs(-2):
                    pool.wait_ge(s_x1, it.done(-2))
                    pool.wait_ge(s_f, it.done(-3))
                    pool.tensor_tensor(x1b[:, :, :], x1[:, :, :],
                                       bias_s[:, :].rearrange("p (o d) -> p o d", o=1).to_broadcast([P, NB, D]),
                                       ALU.add).then_inc(s_x1b, 1)
                if it.runs(1):
                    split_max(it, 0, 1)
                if it.runs(0):
                    mask(it, 1, 0)
                if it.runs(3):
                    rstd(it, ve1, rs1, s_ve1, s_rs1, 3)
                    pool.wait_ge(s_rs1, it.done(3))
                    pool.wait_ge(s_xT, it.done(2))
                    alone(pool, "pool")
                    normalise(it, xa, mv1, rs1, xhat, s_xhat, 3)
                if it.runs(0):
                    mask(it, 2, 0)

            iterate(pool, step)

        @block.scalar
        def _(act):
            def bank6_and_7(it, h):
                if h == 1 and it.runs(2):
                    act.wait_ge(s_xT, it.done(2))
                    act.wait_ge(s_v, it.done(1))
                    act.activation(yT[:, :], bank6[:, 0:SEQ], ACT.Identity, bias=lnb_s[:, :], scale=lnw_s[:, :])\
                        .then_inc(s_yT, 1)
                if h == 1 and it.runs(-1):
                    copy_pv(it, 2, -1)
                if h == 6 and it.runs(-2):
                    act.wait_ge(s_rs2, it.done(-2))
                    act.wait_ge(s_nm2, it.done(-2))
                    act.wait_ge(s_x1T, it.done(-3))
                    act.wait_ge(s_x1b, it.done(-3))
                    for n in range(NB):
                        ins = act.activation(x1[:, n, :], z[:, n, :], ACT.Identity, bias=nm2[:, n:n + 1],
                                             scale=rs2[:, n:n + 1])
                    ins.then_inc(s_x1, 1)
                if h == 3 and it.runs(2):
                    act.wait_ge(s_qk, it.done(2))
                    act.wait_ge(s_stored, it.done(1, STORES))
                    act.activation(parts[:, 0, :, :], bank6[:, :].rearrange("p (a s) -> p a s", a=2), ACT.Copy)\
                        .then_inc(s_p1, 1)
                if h == 4 and it.runs(0):
                    copy_maxT(it, 1, 0, bank7)
                if h == 5 and it.runs(-1):
                    copy_pv(it, 3, -1)
                if h == 5 and it.runs(2):
                    act.wait_ge(s_rest, it.done(2))
                    act.activation(parts[:, 1, :, :], rest[:, :, :], ACT.Copy).then_inc(s_p2, 1)
                if h == 6 and it.runs(2):
                    act.wait_ge(s_v, it.done(2))
                    act.wait_ge(s_pv[GROUPS - 1], it.done(-1))
                    act.wait_ge(s_const2, 2)
                    act.activation(v_ext[it.ring(2)][:, :, :, 0:HD],
                                   bank6[:, 0:SEQ].rearrange("p (n h e) -> p n h e", n=NB, h=HEADS), ACT.Copy)\
                        .then_inc(s_vx, 1)
                if h == 9 and it.runs(-2):
                    act.wait_ge(s_x1T, it.done(-2))
                    act.wait_ge(s_ff, it.done(-3))
                    act.activation(x1T[:, :], bank6[:, 0:SEQ], ACT.Copy).then_inc(s_x1Ts, 1)
                if h == 9 and it.runs(0):
                    copy_pv(it, 0, 0)
                if h == 10 and it.runs(-1):
                    act.wait_ge(s_aT, it.done(-1))
                    act.wait_ge(s_wo, it.done(-2))
                    act.activation(attnT[:, :], bank7[:, 0:SEQ], ACT.Copy).then_inc(s_aTs, 1)
                if h == 12 and it.runs(1):
                    copy_maxT(it, 0, 1, bank6)
                if h == 13 and it.runs(0):
                    copy_pv(it, 1, 0)

            def copy_pv(it, group, offset):
                act.wait_ge(s_pv[group], it.done(offset))
                act.wait_ge(s_ot[(group + 2) % GROUPS], it.done(offset if group >= 2 else offset - 1))
                act.activation(pv_s[group % 2][:, :], pv_bank[group % 2][:, 0:SEQ], ACT.Copy)\
                    .then_inc(s_pvs[group], 1)

            def copy_maxT(it, half, offset, bank):
                act.wait_ge(s_mTp[half], it.done(offset))
                act.wait_ge(s_mrow[half], it.done(offset - 1, MAX_ROWS))
                act.activation(mT[half][:, :], bank[:, :].bitcast(BF16)[0:MAX_PARTS * HALF, 0:SEQ], ACT.Copy)\
                    .then_inc(s_mT[half], 1)

            def step(it):
                for h in range(HEADS):
                    if it.runs(0):
                        act.wait_ge(s_score[h], it.done(0))
                        act.wait_ge(s_pv[h // GROUP], it.done(-1))
                        act.activation(probs[:, h, 0:PW], score_bank[h % 2][:, 0:PW], ACT.Exp, scale=SCALE)\
                            .then_inc(s_exp[h], 1)
                    bank6_and_7(it, h)

            act.wait_ge(s_w, N_W)
            iterate(act, step)

        @block.vector
        def _(dve):
            dve.memset(zero_rows[:, :], 0.0).then_inc(s_zero, 1)
            for t in qx:
                dve.memset(t[64:P, :, :].bitcast(F32), 0.0)
            for t in v_ext:
                dve.memset(t[:, :, :, :], 0.0)
            ins = dve.memset(ones_row[:, :], 1.0)
            ins.then_inc(s_lowc, 1)
            dve.wait_ge(s_lowc, 1)
            for t in v_ext:
                ins = dve.memset(t[:, :, :, HD:HD + 1], 1.0)
            ins.then_inc(s_const2, 1)
            dve.wait_ge(s_low, 1)
            dve.tensor_copy(bias_s[:, :], bank6[:, 0:D])
            dve.tensor_copy(low1[:, :], bank7[0:RANK, 0:D]).then_inc(s_lowc, 1)
            dve.wait_ge(s_low, 2)
            dve.tensor_copy(low2[:, :], bank7[0:UDIM, 0:D]).then_inc(s_lowc, 1)
            dve.wait_ge(s_low, 3)
            dve.tensor_tensor(wf_s[:, :], bank7[:, 0:D], w_raw[:, :], ALU.add).then_inc(s_lowc, 1)
            dve.wait_ge(s_const, N_CONST)

            def stats(source, st, signal):
                for n in range(NB):
                    ins = dve.bn_stats(st[:, n, :], source[:, n, :])
                ins.then_inc(signal, 1)

            def aggregate(st, mv, signal):
                for n in range(NB):
                    ins = dve.bn_aggr(mv[:, n, :], st[:, n, :])
                ins.then_inc(signal, 1)

            def add_eps(mv, ve, signal):
                dve.tensor_scalar(ve[:, :], mv[:, :, 1:2].rearrange("p n o -> p (n o)"), EPS, None, ALU.add)\
                    .then_inc(signal, 1)

            def pvT():
                return bank7[:, 0:SEQ].rearrange("p (n g w) -> p n g w", n=NB, g=GROUP)

            def reciprocal(it, group, offset):
                dve.wait_ge(s_ot[group], it.done(offset))
                dve.reciprocal(rden[:, :, :], pvT()[:, :, :, HD]).then_inc(s_rden[group], 1)

            def divide(it, group, offset):
                dve.wait_ge(s_rden[group], it.done(offset))
                if group == 0:
                    dve.wait_ge(s_aT, it.done(offset - 1))
                o = attn[:, :, group * GROUP * HD:(group + 1) * GROUP * HD].rearrange("p n (g e) -> p n g e", g=GROUP)
                dve.tensor_tensor(o, pvT()[:, :, :, 0:HD],
                                  rden[:, :, :].rearrange("p n (g o) -> p n g o", o=1).to_broadcast([P, NB, GROUP, HD]),
                                  ALU.mult).then_inc(s_norm[group], 1)

            NORMS = {6: (2, -1), 8: (3, -1), 12: (0, 0), 0: (1, -1)}

            def side(it, h):
                if h == 0 and it.runs(-2):
                    dve.wait_ge(s_stat2, it.done(-2))
                    alone(dve, "dve")
                    aggregate(st2, mv2, s_mv2)
                if h == 1 and it.runs(-3):
                    dve.wait_ge(s_mv3, it.done(-3))
                    add_eps(mv3, ve3, s_ve3)
                if h == 1 and it.runs(-2):
                    dve.wait_ge(s_mv2, it.done(-2))
                    add_eps(mv2, ve2, s_ve2)
                if h == 4 and it.runs(-2):
                    dve.wait_ge(s_rs2, it.done(-2))
                    dve.scalar_tensor_tensor(out=nm2[:, :], in0=mv2[:, :, 0:1].rearrange("p n o -> p (n o)"), scalar=-1.0,
                                             in1=rs2[:, :], op0=ALU.mult, op1=ALU.mult).then_inc(s_nm2, 1)
                if h == 4 and it.runs(2):
                    dve.wait_ge(s_p1, it.done(2))
                    dve.wait_ge(s_p3, it.done(1))
                    dve.tensor_tensor(rest[:, :, :], bank6[:, :].rearrange("p (a s) -> p a s", a=2),
                                      parts[:, 0, :, :], ALU.subtract).then_inc(s_rest, 1)
                if h == 8 and it.runs(3):
                    dve.wait_ge(s_xa, it.done(3, 16))
                    stats(xa, st1, s_stat1)
                if h == 9 and it.runs(3):
                    dve.wait_ge(s_stat1, it.done(3))
                    alone(dve, "dve")
                    aggregate(st1, mv1, s_mv1)
                if h == 10 and it.runs(3):
                    dve.wait_ge(s_mv1, it.done(3))
                    add_eps(mv1, ve1, s_ve1)
                if h == 14 and it.runs(-2):
                    dve.wait_ge(s_ff, it.done(-2))
                    dve.wait_ge(s_x1b, it.done(-2))
                    dve.wait_ge(s_y, it.done(-3))
                    dve.tensor_tensor(f[:, :, :], bank6[:, 0:SEQ].rearrange("p (n d) -> p n d", n=NB), x1b[:, :, :],
                                      ALU.add).then_inc(s_f, 1)
                if h == 15 and it.runs(-2):
                    dve.wait_ge(s_f, it.done(-2))
                    stats(f, st3, s_stat3)
                if h == 14 and it.runs(-1):
                    dve.wait_ge(s_wo, it.done(-1))
                    dve.wait_ge(s_xr, it.done(-1, 16))
                    dve.wait_ge(s_x1, it.done(-2))
                    dve.scalar_tensor_tensor(out=z[:, :, :], in0=xr[:, :, :], scalar=2.0,
                                             in1=bank7[:, 0:SEQ].rearrange("p (n d) -> p n d", n=NB),
                                             op0=ALU.mult, op1=ALU.add).then_inc(s_z, 1)
                if h == 0 and it.runs(-3):
                    dve.wait_ge(s_stat3, it.done(-3))
                    alone(dve, "dve")
                    aggregate(st3, mv3, s_mv3)
                if h == 15 and it.runs(-1):
                    dve.wait_ge(s_z, it.done(-1))
                    stats(z, st2, s_stat2)

            def step(it):
                for h in range(HEADS):
                    group, offset = NORMS.get(h, (None, 0))
                    if group is not None and it.runs(offset):
                        reciprocal(it, group, offset)
                    if it.runs(1):
                        half, c = h // HALF, h % HALF
                        dve.wait_ge(s_mscore[h], it.done(1))
                        if c == 0:
                            dve.wait_ge(s_mp2[half], it.done(0))
                        alone(dve, "dve")
                        for n, (a, b) in enumerate(((0, P), (P, PW))):
                            ins = dve.tensor_tensor_reduce(max_bank[h % 2][:, a:b], max_bank[h % 2][:, a:b],
                                                           causal[:, SEQ - (b - a):SEQ], 1.0, LOWEST, ALU.add, ALU.max,
                                                           rowmax[half][:, n, c:c + 1])
                        ins.then_inc(s_mread[h], 1)
                    if group is not None and it.runs(offset):
                        divide(it, group, offset)
                    side(it, h)

            iterate(dve, step)

        @block.tensor
        def _(pe):
            pe.wait_ge(s_w, N_W)
            pe.wait_ge(s_lowc, 1)
            pe.matmul(bank6[:, 0:D], ones_row[:, :], bias_row[:, :], start=True, stop=True)
            pe.matmul(bank7[0:RANK, 0:D], down_s[:, :], daux_s[:, :], start=True, stop=True).then_inc(s_low, 1)
            pe.wait_ge(s_lowc, 2)
            pe.matmul(bank7[0:UDIM, 0:D], up_s[:, :], low1[:, :], start=True, stop=True).then_inc(s_low, 1)
            pe.wait_ge(s_lowc, 3)
            pe.matmul(bank7[:, 0:D], low2[:, :], uaux_s[:, :], start=True, stop=True).then_inc(s_low, 1)
            pe.wait_ge(s_lowc, 4)
            pe.wait_ge(s_const, N_CONST)
            pe.wait_ge(s_const2, 2)

            def max_scores(it, h):
                q, k = qx[it.ring(1)], kx[it.ring(1)]
                if h == 0:
                    pe.wait_ge(s_expand, it.done(1, EXPAND))
                pe.wait_ge(s_mread[(h - 2) % HEADS], it.done(1 if h >= 2 else 0))
                bank = max_bank[h % 2]
                pe.matmul(bank[:, 0:P], q[:, h, 0:P], k[:, h, 0:P], start=True, stop=True)
                pe.matmul(bank[:, P:PW], q[:, h, P:SEQ], k[:, h, 0:SEQ],
                          start=True, stop=True).then_inc(s_mscore[h], 1)

            def scores(it, h):
                q, k = qx[it.ring(0)], kx[it.ring(0)]
                if h % HALF == 0:
                    pe.wait_ge(s_mrow[h // HALF], it.done(0, MAX_ROWS))
                pe.wait_ge(s_exp[(h - 2) % HEADS], it.done(0 if h >= 2 else -1))
                bank = score_bank[h % 2]
                pe.matmul(bank[:, 0:SEQ], k[:, h, 0:P], q[:, h, :], start=True, stop=True)
                pe.matmul(bank[:, SEQ:PW], k[:, h, P:SEQ], q[:, h, P:SEQ],
                          start=True, stop=True).then_inc(s_score[h], 1)

            def pv(it, group, offset, n):
                r = it.ring(offset)
                if n == 0:
                    pe.wait_ge(s_mask[group], it.done(offset))
                    pe.wait_ge(s_pvs[(group + 2) % GROUPS], it.done(offset if group >= 2 else offset - 1))
                    if group == 0:
                        pe.wait_ge(s_vx, it.done(offset))
                for g in range(GROUP):
                    h = GROUP * group + g
                    bank = pv_bank[group % 2][VW * g:VW * g + VW, :]
                    ins = pe.matmul(bank[:, n * P:SEQ], v_ext[r][:, n, h, :],
                                    probs[:, h, 0:SEQ] if n == 0 else probs[:, h, SEQ:PW],
                                    start=(n == 0), stop=(n == NB - 1), skip_group_check=True)
                if n == NB - 1:
                    ins.then_inc(s_pv[group], 1)

            def transpose2(bank, source, signal):
                for n in range(NB):
                    ins = pe.transpose(bank[:, n * P:n * P + P], source(n), ident[:, :])
                ins.then_inc(signal, 1)

            def pv_transpose(it, group, offset):
                pe.wait_ge(s_pvs[group], it.done(offset))
                transpose2(bank7, lambda n: pv_s[group % 2][:, n * P:n * P + P], s_ot[group])

            def max_transpose(it, half, offset, bank):
                pe.wait_ge(s_mp2[half], it.done(offset))
                for n in range(NB):
                    ins = pe.transpose(bank[:, :].bitcast(BF16)[0:MAX_PARTS * HALF, n * P:n * P + P],
                                       mpart[half][:, n, :, :].rearrange("p a h -> p (a h)"), ident_b[:, :])
                ins.then_inc(s_mTp[half], 1)

            def in_bank6(it, h):
                if h == 0 and it.runs(2):
                    pe.wait_ge(s_f, it.done(-3))
                    pe.wait_ge(s_mT[0], it.done(0))
                    pe.wait_ge(s_vx, it.done(1))
                    pe.wait_ge(s_xhat, it.done(2))
                    transpose2(bank6, lambda n: xhat[:, n, :], s_xT)
                if h == 2 and it.runs(2):
                    pe.wait_ge(s_yT, it.done(2))
                    pe.matmul(bank6[:, 0:SEQ], wq_s[:, :], yT[:, :], start=True, stop=True)
                    pe.matmul(bank6[:, SEQ:2 * SEQ], wk_s[:, :], yT[:, :], start=True, stop=True).then_inc(s_qk, 1)
                if h == 5 and it.runs(2):
                    pe.wait_ge(s_rest, it.done(2))
                    for n in range(NB):
                        ins = pe.matmul(bank6[:, n * D:n * D + D], yT[:, n * P:n * P + P], wv_s[:, :],
                                        start=True, stop=True)
                    ins.then_inc(s_v, 1)
                if h == 8 and it.runs(-2):
                    if it.runs(2):
                        pe.wait_ge(s_vx, it.done(2))
                    else:
                        pe.wait_ge(s_mT[0], min(it.done(0), BATCHES))
                        pe.wait_ge(s_vx, BATCHES)
                        pe.wait_ge(s_f, it.done(-3))
                    pe.wait_ge(s_x1, it.done(-2))
                    transpose2(bank6, lambda n: x1[:, n, :], s_x1T)
                if h == 11 and it.runs(1):
                    pe.wait_ge(s_vx, it.done(2) if it.runs(2) else BATCHES)
                    pe.wait_ge(s_x1Ts, it.done(-2))
                    max_transpose(it, 0, 1, bank6)
                if h == 13 and it.runs(-2):
                    pe.wait_ge(s_mT[0], it.done(1) if it.runs(1) else BATCHES)
                    pe.wait_ge(s_x1Ts, it.done(-2))
                    for n in range(NB):
                        ins = pe.matmul(bank6[:, n * D:n * D + D], x1T[:, n * P:n * P + P], wf_s[:, :],
                                        start=True, stop=True)
                    ins.then_inc(s_ff, 1)

            def in_bank7(it, h):
                if h == 3 and it.runs(0):
                    pe.wait_ge(s_norm[1], it.done(-1))
                    max_transpose(it, 1, 0, bank7)
                if h == 5 and it.runs(-1):
                    pe.wait_ge(s_norm[1], it.done(-1))
                    pe.wait_ge(s_mT[1], it.done(0) if it.runs(0) else BATCHES)
                    pv_transpose(it, 2, -1)
                if h == 7 and it.runs(-1):
                    pe.wait_ge(s_norm[2], it.done(-1))
                    pv_transpose(it, 3, -1)
                if h == 9 and it.runs(-1):
                    pe.wait_ge(s_norm[3], it.done(-1))
                    transpose2(bank7, lambda n: attn[:, n, :], s_aT)
                if h == 11 and it.runs(0):
                    pe.wait_ge(s_mT[1], it.done(0))
                    pe.wait_ge(s_aTs, it.done(-1))
                    pv_transpose(it, 0, 0)
                if h == 13 and it.runs(-1):
                    pe.wait_ge(s_norm[0], it.done(0) if it.runs(0) else BATCHES)
                    pe.wait_ge(s_aTs, it.done(-1))
                    for n in range(NB):
                        ins = pe.matmul(bank7[:, n * D:n * D + D], attnT[:, n * P:n * P + P], wo_s[:, :],
                                        start=True, stop=True)
                    ins.then_inc(s_wo, 1)
                if h == 15 and it.runs(0):
                    pe.wait_ge(s_norm[0], it.done(0))
                    pe.wait_ge(s_z, it.done(-1))
                    pv_transpose(it, 1, 0)

            PVS = {3: (3, -1, 0), 4: (3, -1, 1), 7: (0, 0, 0), 8: (0, 0, 1), 11: (1, 0, 0), 12: (1, 0, 1),
                   15: (2, 0, 0), 0: (2, -1, 1)}

            def step(it):
                for h in range(HEADS):
                    if it.runs(1):
                        max_scores(it, h)
                    if it.runs(0):
                        scores(it, h)
                    if h in PVS:
                        group, offset, n = PVS[h]
                        if it.runs(offset):
                            pv(it, group, offset, n)
                    in_bank6(it, h)
                    in_bank7(it, h)

            iterate(pe, step)


def kernel(**inputs):
    import numpy as np
    import concourse.bacc as bacc
    from concourse.bass_utils import run_bass_kernel_spmd

    def of(name):
        return np.asarray(inputs[name])

    def heads_inner(w):
        return w.transpose(1, 2, 0).reshape(D, D)

    arrays = {
        "x": of("L0_attn_x"),
        "ln_w": of("L0_attn_ln_w").reshape(D, 1),
        "ln_b": of("L0_attn_ln_b").reshape(D, 1),
        "wq": heads_inner(of("L0_attn_wq")),
        "wk": heads_inner(of("L0_attn_wk")),
        "wv": of("L0_attn_wv").transpose(1, 0, 2).reshape(D, D),
        "wo": of("L0_attn_wo"),
        "w_t": of("L0_ffn_W").T,
        "bias": of("L0_ffn_b").reshape(1, D),
        "down_t": of("L0_ffn_lora_down").T,
        "up_t": of("L0_ffn_lora_up").T,
        "down_aux": of("L0_ffn_down_aux"),
        "up_aux_t": of("L0_ffn_up_aux").T,
    }
    arrays = {f"in_{k}": np.ascontiguousarray(a) for k, a in arrays.items()}
    nc = bacc.Bacc("TRN2", target_bir_lowering=False, num_devices=1)
    args = [nc.dram_tensor(k, a.shape, mybir.dt.from_np(a.dtype), kind="ExternalInput").ap() for k, a in arrays.items()]
    out = nc.dram_tensor("out", (BATCHES, SEQ, D), F32, kind="ExternalOutput").ap()
    build(nc, *args, out)
    r = run_bass_kernel_spmd(nc, [arrays], core_ids=[0])
    return r.results[0]["out"]
```

```python
from contextlib import ExitStack

import concourse.bass as bass
from concourse import mybir

F32 = mybir.dt.float32
BF16 = mybir.dt.bfloat16
ALU = mybir.AluOpType
ACT = mybir.ActivationFunctionType

P = 128
BATCHES, SEQ, D = 32, 256, 128
HEADS = 16
HD = D // HEADS
NB = SEQ // P
PARTS = 3
PART_ROWS = PARTS * HD
SPLIT_ROWS = PARTS * PART_ROWS
MAX_PARTS = 2
SCORE_ROWS = SPLIT_ROWS + MAX_PARTS
GROUP = 4
GROUPS = HEADS // GROUP
HALF = HEADS // 2
VW = P // GROUP
PW = SEQ + P
EPS = 1e-5
SCALE = float(HD) ** -0.5
LOWEST = -3.0e38
RING = 3
FIRST, LAST = -4, BATCHES + 2
LOOP_FROM = 4
LOOP_TO = LOOP_FROM + (BATCHES - 5 - LOOP_FROM) // RING * RING
RANK, DDIM, UDIM = 4, 100, 50


class Iteration:

    def __init__(self, eng, base, u, cache):
        self.eng, self.base, self.u, self.cache = eng, base, u, cache
        self.static = isinstance(base, int)

    def runs(self, offset):
        return not self.static or 0 <= self.base + self.u + offset < BATCHES

    def batch(self, offset):
        return self.base + (self.u + offset)

    def ring(self, offset):
        return ((self.base if self.static else LOOP_FROM) + self.u + offset) % RING

    def done(self, offset, per=1):
        c = self.u + offset + 1
        if self.static:
            return per * min(max(0, self.base + c), BATCHES)
        if (c, per) not in self.cache:
            self.cache[c, per] = self.eng.snap((self.base + c) * per if per > 1 else self.base + c)
        return self.cache[c, per]


def iterate(eng, step):
    for it in range(FIRST, LOOP_FROM):
        step(Iteration(eng, it, 0, {}))
    with eng.Fori(LOOP_FROM, LOOP_TO - RING + 1, RING) as base:
        cache = {}
        for u in range(RING):
            step(Iteration(eng, base, u, cache))
    for it in range(LOOP_TO, LAST + 1):
        step(Iteration(eng, it, 0, {}))


def build(nc, x, ln_w, ln_b, wq, wk, wv, wo, w_t, bias, down_t, up_t, down_aux, up_aux_t, out):
    with ExitStack() as ctx:
        def sb(name, shape, dt=F32):
            return ctx.enter_context(nc.sbuf_tensor(name, shape, dt))

        def sem(name):
            return ctx.enter_context(nc.semaphore(name))

        def sems(name, n):
            return [sem(f"{name}{i}") for i in range(n)]

        max_bank = [ctx.enter_context(nc.psum_tensor(f"max_bank{i}", [P, 512], F32)) for i in range(2)]
        score_bank = [ctx.enter_context(nc.psum_tensor(f"score_bank{i}", [P, 512], F32)) for i in range(2)]
        pv_bank = [ctx.enter_context(nc.psum_tensor(f"pv_bank{i}", [P, 512], F32)) for i in range(2)]
        bank6 = ctx.enter_context(nc.psum_tensor("bank6", [P, 512], F32))
        bank7 = ctx.enter_context(nc.psum_tensor("bank7", [P, 512], F32))

        ident = sb("ident", [P, P])
        ident_b = sb("ident_b", [P, P], BF16)
        causal = sb("causal", [P, SEQ])
        ones_row = sb("ones_row", [1, P])
        wq_s, wk_s, wv_s, wo_s = (sb(n, [P, D]) for n in ("wq_s", "wk_s", "wv_s", "wo_s"))
        wf_s = sb("wf_s", [P, D])
        w_raw = sb("w_raw", [P, D])
        lnw_s, lnb_s = sb("lnw_s", [P, 1]), sb("lnb_s", [P, 1])
        bias_row = sb("bias_row", [1, D])
        bias_s = sb("bias_s", [P, D])
        down_s, up_s = sb("down_s", [DDIM, RANK]), sb("up_s", [RANK, UDIM])
        daux_s, uaux_s = sb("daux_s", [DDIM, D]), sb("uaux_s", [UDIM, D])
        low1, low2 = sb("low1", [RANK, D]), sb("low2", [UDIM, D])

        zero_rows = sb("zero_rows", [MAX_PARTS * HEADS, SEQ], BF16)
        xa = sb("xa", [P, NB, D])
        power = sb("power", [P, NB])
        st1, mv1, ve1, rs1 = sb("st1", [P, NB, 6]), sb("mv1", [P, NB, 2]), sb("ve1", [P, NB]), sb("rs1", [P, NB])
        xhat = sb("xhat", [P, NB, D])
        yT = sb("yT", [P, SEQ])
        parts = sb("parts", [P, PARTS, 2, SEQ], BF16)
        rest = sb("rest", [P, 2, SEQ])
        v_ext = [sb(f"v_ext{i}", [P, NB, HEADS, VW]) for i in range(RING)]
        qx = [sb(f"qx{i}", [P, HEADS, SEQ], BF16) for i in range(RING)]
        kx = [sb(f"kx{i}", [P, HEADS, SEQ], BF16) for i in range(RING)]
        rowmax = [sb(f"rowmax{i}", [P, NB, HALF]) for i in range(2)]
        mpart = [sb(f"mpart{i}", [P, NB, MAX_PARTS, HALF], BF16) for i in range(2)]
        mT = [sb(f"mT{i}", [MAX_PARTS * HALF, SEQ], BF16) for i in range(2)]
        probs = sb("probs", [P, HEADS, 2 * SEQ])
        pv_s = [sb(f"pv_s{i}", [P, SEQ]) for i in range(2)]
        rden = [sb(f"rden{i}", [P, NB, GROUP]) for i in range(2)]
        attn = sb("attn", [P, NB, D])
        attnT = sb("attnT", [P, SEQ])
        xr = sb("xr", [P, NB, D])
        z = sb("z", [P, NB, D])
        st2, mv2, ve2, rs2 = sb("st2", [P, NB, 6]), sb("mv2", [P, NB, 2]), sb("ve2", [P, NB]), sb("rs2", [P, NB])
        nm2, nm3 = sb("nm2", [P, NB]), sb("nm3", [P, NB])
        x1 = sb("x1", [P, NB, D])
        x1b = sb("x1b", [P, NB, D])
        x1T = sb("x1T", [P, SEQ])
        f = sb("f", [P, NB, D])
        st3, mv3, ve3, rs3 = sb("st3", [P, NB, 6]), sb("mv3", [P, NB, 2]), sb("ve3", [P, NB]), sb("rs3", [P, NB])
        y = sb("y", [P, NB, D])

        q_rows = nc.dram_tensor("q_rows", [(PART_ROWS + MAX_PARTS) * HEADS, SEQ], BF16).ap()
        k_rows = nc.dram_tensor("k_rows", [(2 * PARTS - 1) * P, SEQ], BF16).ap()

        s_w = sem("weights_loaded")
        s_const = sem("constants_made")
        s_zero = sem("zero_rows_made_and_stored")
        s_const2 = sem("buffers_filled")
        s_low = sem("low_rank_product")
        s_lowc = sem("low_rank_copied")
        s_xa, s_xr, s_st = sem("xa_loaded"), sem("xr_loaded"), sem("y_stored")
        s_nm3 = sem("shift3")
        s_ve1, s_ve2, s_ve3 = (sem(f"variance_plus_eps{i}") for i in (1, 2, 3))
        s_stat1, s_mv1, s_rs1, s_xhat = sem("stats1"), sem("mean_var1"), sem("rstd1"), sem("xhat_ready")
        s_xT, s_yT = sem("xT_in_bank6"), sem("yT_ready")
        s_qk, s_p1, s_rest, s_p2, s_p3 = (sem("qk_in_bank6"), sem("parts1_ready"), sem("rest_ready"),
                                          sem("parts2_ready"), sem("parts3_ready"))
        s_q_stored = sem("q_stored")
        s_stored = sem("k_stored")
        s_expand = sem("heads_expanded")
        s_v, s_vx = sem("v_in_bank6"), sem("v_ext_ready")
        s_mscore, s_mread = sems("max_scores_in_bank_h", HEADS), sems("row_max_of_h", HEADS)
        s_mp1, s_mp2 = sems("max_part1_", 2), sems("max_part2_", 2)
        s_mTp, s_mT = sems("maxT_in_bank", 2), sems("maxT_ready", 2)
        s_mrow = sems("max_rows_loaded", 2)
        s_score, s_exp = sems("scores_in_bank_h", HEADS), sems("exp_of_h", HEADS)
        s_mask = sems("probs_masked_group", GROUPS)
        s_pv, s_pvs = sems("pv_in_bank_group", GROUPS), sems("pv_copied_group", GROUPS)
        s_ot, s_rden, s_norm = sems("pvT_in_bank_group", GROUPS), sems("rden_group", GROUPS), sems("attn_group", GROUPS)
        s_aT, s_aTs = sem("attnT_in_bank7"), sem("attnT_ready")
        s_wo, s_z = sem("out_in_bank7"), sem("z_ready")
        s_stat2, s_mv2, s_rs2, s_nm2, s_x1 = sem("stats2"), sem("mean_var2"), sem("rstd2"), sem("shift2"), sem("x1_ready")
        s_x1b, s_x1T, s_x1Ts = sem("x1_plus_bias"), sem("x1T_in_bank6"), sem("x1T_ready")
        s_ff, s_f = sem("linear_in_bank6"), sem("f_ready")
        s_stat3, s_mv3, s_rs3, s_y = sem("stats3"), sem("mean_var3"), sem("rstd3"), sem("y_ready")

        weights = [(wq_s, wq), (wk_s, wk), (wv_s, wv), (wo_s, wo), (w_raw, w_t), (lnw_s, ln_w), (lnb_s, ln_b),
                   (bias_row, bias), (down_s, down_t), (up_s, up_t), (daux_s, down_aux), (uaux_s, up_aux_t)]
        N_W = 16 * len(weights)
        N_CONST = 7
        EXPAND = 16 * 2 * PARTS
        STORES = 16 * 2
        MAX_ROWS = 16 * MAX_PARTS

        s_passed = {e: sem(f"waits_passed_{e}") for e in ("sp", "pool", "dve")}

        def alone(eng, name):
            eng.sem_inc(s_passed[name], 1)

        block = ctx.enter_context(nc.Block())

        def rows(dram, batch):
            return dram[bass.ds(batch, 1), :, :].rearrange("o (n p) d -> p (o n) d", p=P)

        @block.sync
        def _(sp):
            sp.dma_start(xa[:, :, :], rows(x, 0)).then_inc(s_xa, 16)
            for tile, dram in weights:
                sp.dma_start(tile[:, :], dram[:, :]).then_inc(s_w, 16)
            sp.wait_ge(s_zero, 1)
            sp.dma_start(q_rows[PARTS * P:, :], zero_rows[:, :]).then_inc(s_zero, 16)
            sp.wait_ge(s_zero, 17)
            sp.wait_ge(s_const2, 2)

            def store_parts(it):
                for dram, which, first, n, stored in ((q_rows, 0, 0, PARTS, s_q_stored), (k_rows, 1, 0, PARTS, s_stored),
                                                      (k_rows, 1, PARTS, PARTS - 1, s_stored)):
                    sp.dma_start(dram[first * P:(first + n) * P, :].rearrange("(i p) s -> p i s", p=P),
                                 parts[:, 0:n, which, :]).then_inc(stored, 16)

            def expand(it):
                r = it.ring(2)
                q, k = (t.rearrange("(r h) s -> r h s", h=HEADS) for t in (q_rows, k_rows))
                sp.wait_ge(s_q_stored, it.done(2, 16))
                for turn in range(PARTS):
                    a, n = turn * PART_ROWS, PART_ROWS + (MAX_PARTS if turn == PARTS - 1 else 0)
                    sp.dma_start(qx[r][a:a + n, :, :], q[0:n, :, :]).then_inc(s_expand, 16)
                sp.wait_ge(s_stored, it.done(2, STORES))
                for turn in range(PARTS):
                    a = turn * PART_ROWS
                    sp.dma_start(kx[r][a:a + PART_ROWS, :, :],
                                 k[turn * HD:turn * HD + PART_ROWS, :, :]).then_inc(s_expand, 16)

            def max_rows(it, half, offset):
                sp.wait_ge(s_mT[half], it.done(offset))
                for part in range(MAX_PARTS):
                    sp.dma_start(qx[it.ring(offset)][SPLIT_ROWS + part:SPLIT_ROWS + part + 1,
                                                     half * HALF:(half + 1) * HALF, :],
                                 mT[half][part * HALF:(part + 1) * HALF, :]).then_inc(s_mrow[half], 16)

            def step(it):
                if it.runs(0):
                    max_rows(it, 1, 0)
                if it.runs(2):
                    sp.wait_ge(s_expand, it.done(1, EXPAND))
                    alone(sp, "sp")
                    sp.wait_ge(s_p3, it.done(2))
                    store_parts(it)
                    sp.wait_ge(s_score[HEADS - 1], it.done(-1))
                    alone(sp, "sp")
                    expand(it)
                if it.runs(1):
                    max_rows(it, 0, 1)
                if it.runs(0):
                    sp.wait_ge(s_z, it.done(-1))
                    sp.dma_start(xr[:, :, :], rows(x, it.batch(0))).then_inc(s_xr, 16)
                if it.runs(-3):
                    sp.wait_ge(s_y, it.done(-3))
                    sp.dma_start(rows(out, it.batch(-3)), y[:, :, :]).then_inc(s_st, 16)

                if it.runs(5):
                    sp.wait_ge(s_xhat, it.done(4))
                    sp.dma_start(xa[:, :, :], rows(x, it.batch(5))).then_inc(s_xa, 16)

            iterate(sp, step)
            sp.wait_ge(s_st, 16 * BATCHES)

        @block.gpsimd
        def _(pool):
            for t in kx:
                ins = pool.memset(t[:, :, :], -1.0)
            ins.then_inc(s_const2, 1)
            pool.memset(ident[:, :], 0.0).then_inc(s_const, 1)
            pool.memset(ident_b[:, :], 0.0).then_inc(s_const, 1)
            pool.memset(causal[:, :], 0.0).then_inc(s_const, 1)
            pool.memset(power[:, :], -0.5).then_inc(s_const, 1)
            pool.wait_ge(s_const, 4)
            for m in (ident, ident_b):
                pool.affine_select(out=m[:, :], in_=m[:, :], compare_op=ALU.not_equal, fill=1.0,
                                   base=0, pattern=[[-1, P]], channel_multiplier=1).then_inc(s_const, 1)
            pool.affine_select(out=causal[:, P:SEQ], in_=causal[:, P:SEQ], compare_op=ALU.is_ge, fill=LOWEST,
                               base=0, pattern=[[-1, P]], channel_multiplier=1).then_inc(s_const, 1)

            def split_max(it, half, offset):
                pool.wait_ge(s_mread[half * HALF + HALF - 1], it.done(offset))
                pool.wait_ge(s_mTp[half], it.done(offset - 1))
                alone(pool, "pool")
                pool.tensor_copy(mpart[half][:, :, 0, :], rowmax[half][:, :, :]).then_inc(s_mp1[half], 1)
                pool.wait_ge(s_mp1[half], it.done(offset))
                pool.tensor_tensor(mpart[half][:, :, 1, :], rowmax[half][:, :, :], mpart[half][:, :, 0, :],
                                   ALU.subtract).then_inc(s_mp2[half], 1)

            def mask(it, group, offset):
                for h in range(GROUP * group, GROUP * group + GROUP):
                    pool.wait_ge(s_exp[h], it.done(offset))
                alone(pool, "pool")
                t = probs[:, GROUP * group:GROUP * group + GROUP, :].rearrange("p h (c s) -> p (h c) s", s=SEQ)[:, :, 0:P]
                pool.affine_select(out=t, in_=t, compare_op=ALU.is_ge, fill=0.0, base=0,
                                   pattern=[[0, GROUP * NB], [1, P]], channel_multiplier=-1)\
                    .then_inc(s_mask[group], 1)

            def rstd(it, ve, rs, added, signal, offset):
                pool.wait_ge(added, it.done(offset))
                pool.tensor_tensor(rs[:, :], ve[:, :], power[:, :], ALU.pow).then_inc(signal, 1)

            def step(it):
                if it.runs(0):
                    split_max(it, 1, 0)
                if it.runs(-1):
                    mask(it, GROUPS - 1, -1)
                if it.runs(-2):
                    rstd(it, ve2, rs2, s_ve2, s_rs2, -2)
                if it.runs(0):
                    mask(it, 0, 0)
                if it.runs(2):
                    pool.wait_ge(s_p2, it.done(2))
                    pool.tensor_tensor(parts[:, 2, :, :], rest[:, :, :], parts[:, 1, :, :],
                                       ALU.subtract).then_inc(s_p3, 1)
                if it.runs(1):
                    split_max(it, 0, 1)
                if it.runs(0):
                    mask(it, 1, 0)
                if it.runs(-2):
                    pool.wait_ge(s_x1, it.done(-2))
                    pool.wait_ge(s_f, it.done(-3))
                    pool.tensor_tensor(x1b[:, :, :], x1[:, :, :],
                                       bias_s[:, :].rearrange("p (o d) -> p o d", o=1).to_broadcast([P, NB, D]),
                                       ALU.add).then_inc(s_x1b, 1)
                if it.runs(0):
                    mask(it, 2, 0)
                if it.runs(-3):
                    rstd(it, ve3, rs3, s_ve3, s_rs3, -3)
                if it.runs(4):
                    rstd(it, ve1, rs1, s_ve1, s_rs1, 4)
                if it.runs(4):
                    pool.wait_ge(s_rs1, it.done(4))
                    pool.wait_ge(s_xT, it.done(3))
                    alone(pool, "pool")
                    for n in range(NB):
                        ins = pool.tensor_scalar(xhat[:, n, :], xa[:, n, :], mv1[:, n, 0:1], rs1[:, n:n + 1],
                                                 ALU.subtract, ALU.mult)
                    ins.then_inc(s_xhat, 1)

            iterate(pool, step)

        @block.scalar
        def _(act):
            def bank6_and_7(it, h):
                if h == 14 and it.runs(3):
                    act.wait_ge(s_xT, it.done(3))
                    act.wait_ge(s_v, it.done(2))
                    act.activation(yT[:, :], bank6[:, 0:SEQ], ACT.Identity, bias=lnb_s[:, :], scale=lnw_s[:, :])\
                        .then_inc(s_yT, 1)
                if h == 1 and it.runs(-1):
                    copy_pv(it, 2, -1)
                if h == 5 and it.runs(-2):
                    act.wait_ge(s_nm2, it.done(-2))
                    act.wait_ge(s_x1T, it.done(-3))
                    act.wait_ge(s_x1b, it.done(-3))
                    for n in range(NB):
                        ins = act.activation(x1[:, n, :], z[:, n, :], ACT.Identity, bias=nm2[:, n:n + 1],
                                             scale=rs2[:, n:n + 1])
                    ins.then_inc(s_x1, 1)
                if h == 1 and it.runs(2):
                    act.wait_ge(s_qk, it.done(2))
                    act.wait_ge(s_q_stored, it.done(1, 16))
                    act.wait_ge(s_stored, it.done(1, STORES))
                    act.activation(parts[:, 0, :, :], bank6[:, :].rearrange("p (a s) -> p a s", a=2), ACT.Copy)\
                        .then_inc(s_p1, 1)
                if h == 3 and it.runs(0):
                    copy_maxT(it, 1, 0, bank7)
                if h == 5 and it.runs(-1):
                    copy_pv(it, 3, -1)
                if h == 3 and it.runs(2):
                    act.wait_ge(s_rest, it.done(2))
                    act.activation(parts[:, 1, :, :], rest[:, :, :], ACT.Copy).then_inc(s_p2, 1)
                if h == 5 and it.runs(2):
                    act.wait_ge(s_v, it.done(2))
                    act.wait_ge(s_pv[GROUPS - 1], it.done(-1))
                    act.wait_ge(s_const2, 2)
                    act.activation(v_ext[it.ring(2)][:, :, :, 0:HD],
                                   bank6[:, 0:SEQ].rearrange("p (n h e) -> p n h e", n=NB, h=HEADS), ACT.Copy)\
                        .then_inc(s_vx, 1)
                if h == 8 and it.runs(-2):
                    act.wait_ge(s_x1T, it.done(-2))
                    act.wait_ge(s_ff, it.done(-3))
                    act.activation(x1T[:, :], bank6[:, 0:SEQ], ACT.Copy).then_inc(s_x1Ts, 1)
                if h == 9 and it.runs(0):
                    copy_pv(it, 0, 0)
                if h == 11 and it.runs(-1):
                    act.wait_ge(s_aT, it.done(-1))
                    act.wait_ge(s_wo, it.done(-2))
                    act.activation(attnT[:, :], bank7[:, 0:SEQ], ACT.Copy).then_inc(s_aTs, 1)
                if h == 11 and it.runs(1):
                    copy_maxT(it, 0, 1, bank6)
                if h == 13 and it.runs(0):
                    copy_pv(it, 1, 0)

                if h == 15 and it.runs(-3):
                    act.wait_ge(s_nm3, it.done(-3))
                    act.wait_ge(s_st, it.done(-4, 16))
                    for n in range(NB):
                        ins = act.activation(y[:, n, :], f[:, n, :], ACT.Identity, bias=nm3[:, n:n + 1],
                                             scale=rs3[:, n:n + 1])
                    ins.then_inc(s_y, 1)

            def copy_pv(it, group, offset):
                act.wait_ge(s_pv[group], it.done(offset))
                act.wait_ge(s_ot[(group + 2) % GROUPS], it.done(offset if group >= 2 else offset - 1))
                act.activation(pv_s[group % 2][:, :], pv_bank[group % 2][:, 0:SEQ], ACT.Copy)\
                    .then_inc(s_pvs[group], 1)

            def copy_maxT(it, half, offset, bank):
                act.wait_ge(s_mTp[half], it.done(offset))
                act.wait_ge(s_mrow[half], it.done(offset - 1, MAX_ROWS))
                act.activation(mT[half][:, :], bank[:, :].bitcast(BF16)[0:MAX_PARTS * HALF, 0:SEQ], ACT.Copy)\
                    .then_inc(s_mT[half], 1)

            def step(it):
                for h in range(HEADS):
                    if it.runs(0):
                        act.wait_ge(s_score[h], it.done(0))
                        act.wait_ge(s_pv[h // GROUP], it.done(-1))
                        act.activation(probs[:, h, 0:PW], score_bank[h % 2][:, 0:PW], ACT.Exp, scale=SCALE)\
                            .then_inc(s_exp[h], 1)
                    bank6_and_7(it, h)

            act.wait_ge(s_w, N_W)
            iterate(act, step)

        @block.vector
        def _(dve):
            dve.memset(zero_rows[:, :], 0.0).then_inc(s_zero, 1)
            for t in qx:
                dve.memset(t[64:P, :, :].bitcast(F32), 0.0)
            for t in v_ext:
                dve.memset(t[:, :, :, :], 0.0)
            ins = dve.memset(ones_row[:, :], 1.0)
            ins.then_inc(s_lowc, 1)
            dve.wait_ge(s_lowc, 1)
            for t in v_ext:
                ins = dve.memset(t[:, :, :, HD:HD + 1], 1.0)
            ins.then_inc(s_const2, 1)
            dve.wait_ge(s_low, 1)
            dve.tensor_copy(bias_s[:, :], bank6[:, 0:D])
            dve.tensor_copy(low1[:, :], bank7[0:RANK, 0:D]).then_inc(s_lowc, 1)
            dve.wait_ge(s_low, 2)
            dve.tensor_copy(low2[:, :], bank7[0:UDIM, 0:D]).then_inc(s_lowc, 1)
            dve.wait_ge(s_low, 3)
            dve.tensor_tensor(wf_s[:, :], bank7[:, 0:D], w_raw[:, :], ALU.add).then_inc(s_lowc, 1)
            dve.wait_ge(s_const, N_CONST)

            def stats(source, st, signal):
                for n in range(NB):
                    ins = dve.bn_stats(st[:, n, :], source[:, n, :])
                ins.then_inc(signal, 1)

            def aggregate(st, mv, signal):
                for n in range(NB):
                    ins = dve.bn_aggr(mv[:, n, :], st[:, n, :])
                ins.then_inc(signal, 1)

            def add_eps(mv, ve, signal):
                dve.tensor_scalar(ve[:, :], mv[:, :, 1:2].rearrange("p n o -> p (n o)"), EPS, None, ALU.add)\
                    .then_inc(signal, 1)

            def pvT(group):
                return pv_bank[group % 2][:, SEQ:2 * SEQ].rearrange("p (n g w) -> p n g w", n=NB, g=GROUP)

            def reciprocal(it, group, offset):
                dve.wait_ge(s_ot[group], it.done(offset))
                dve.reciprocal(rden[group % 2][:, :, :], pvT(group)[:, :, :, HD]).then_inc(s_rden[group], 1)

            def divide(it, group, offset):
                dve.wait_ge(s_rden[group], it.done(offset))
                if group == 0:
                    dve.wait_ge(s_aT, it.done(offset - 1))
                o = attn[:, :, group * GROUP * HD:(group + 1) * GROUP * HD].rearrange("p n (g e) -> p n g e", g=GROUP)
                dve.tensor_tensor(o, pvT(group)[:, :, :, 0:HD],
                                  rden[group % 2][:, :, :].rearrange("p n (g o) -> p n g o", o=1).to_broadcast([P, NB, GROUP, HD]),
                                  ALU.mult).then_inc(s_norm[group], 1)

            NORMS = {4: (2, -1), 8: (3, -1), 12: (0, 0), 0: (1, -1)}

            def shift(mv, rs, nm, signal):
                dve.scalar_tensor_tensor(out=nm[:, :], in0=mv[:, :, 0:1].rearrange("p n o -> p (n o)"), scalar=-1.0,
                                         in1=rs[:, :], op0=ALU.mult, op1=ALU.mult).then_inc(signal, 1)

            def side(it, h):
                if h == 15 and it.runs(-1):
                    dve.wait_ge(s_wo, it.done(-1))
                    dve.wait_ge(s_xr, it.done(-1, 16))
                    dve.wait_ge(s_x1, it.done(-2))
                    dve.scalar_tensor_tensor(out=z[:, :, :], in0=xr[:, :, :], scalar=2.0,
                                             in1=bank7[:, 0:SEQ].rearrange("p (n d) -> p n d", n=NB),
                                             op0=ALU.mult, op1=ALU.add).then_inc(s_z, 1)
                if h == 0 and it.runs(-2):
                    dve.wait_ge(s_z, it.done(-2))
                    stats(z, st2, s_stat2)
                if h == 1 and it.runs(-2):
                    dve.wait_ge(s_stat2, it.done(-2))
                    alone(dve, "dve")
                    aggregate(st2, mv2, s_mv2)
                if h == 2 and it.runs(-2):
                    dve.wait_ge(s_mv2, it.done(-2))
                    add_eps(mv2, ve2, s_ve2)
                if h == 4 and it.runs(-2):
                    dve.wait_ge(s_rs2, it.done(-2))
                    shift(mv2, rs2, nm2, s_nm2)
                if h == 2 and it.runs(2):
                    dve.wait_ge(s_p1, it.done(2))
                    dve.wait_ge(s_p3, it.done(1))
                    dve.tensor_tensor(rest[:, :, :], bank6[:, :].rearrange("p (a s) -> p a s", a=2),
                                      parts[:, 0, :, :], ALU.subtract).then_inc(s_rest, 1)
                if h == 7 and it.runs(-3):
                    dve.wait_ge(s_ff, it.done(-3))
                    dve.wait_ge(s_x1b, it.done(-3))
                    dve.wait_ge(s_y, it.done(-4))
                    dve.tensor_tensor(f[:, :, :], bank7[:, 0:SEQ].rearrange("p (n d) -> p n d", n=NB), x1b[:, :, :],
                                      ALU.add).then_inc(s_f, 1)
                if h == 9 and it.runs(-3):
                    dve.wait_ge(s_f, it.done(-3))
                    stats(f, st3, s_stat3)
                if h == 10 and it.runs(-3):
                    dve.wait_ge(s_stat3, it.done(-3))
                    alone(dve, "dve")
                    aggregate(st3, mv3, s_mv3)
                if h == 11 and it.runs(-3):
                    dve.wait_ge(s_mv3, it.done(-3))
                    add_eps(mv3, ve3, s_ve3)
                if h == 14 and it.runs(-3):
                    dve.wait_ge(s_rs3, it.done(-3))
                    shift(mv3, rs3, nm3, s_nm3)
                if h == 8 and it.runs(4):
                    dve.wait_ge(s_xa, it.done(4, 16))
                    stats(xa, st1, s_stat1)
                if h == 12 and it.runs(4):
                    dve.wait_ge(s_stat1, it.done(4))
                    alone(dve, "dve")
                    aggregate(st1, mv1, s_mv1)
                if h == 13 and it.runs(4):
                    dve.wait_ge(s_mv1, it.done(4))
                    add_eps(mv1, ve1, s_ve1)

            def step(it):
                for h in range(HEADS):
                    group, offset = NORMS.get(h, (None, 0))
                    if group is not None and it.runs(offset):
                        reciprocal(it, group, offset)
                    if it.runs(1):
                        half, c = h // HALF, h % HALF
                        dve.wait_ge(s_mscore[h], it.done(1))
                        if c == 0:
                            dve.wait_ge(s_mp2[half], it.done(0))
                        alone(dve, "dve")
                        for n, (a, b) in enumerate(((0, P), (P, PW))):
                            ins = dve.tensor_tensor_reduce(max_bank[h % 2][:, a:b], max_bank[h % 2][:, a:b],
                                                           causal[:, SEQ - (b - a):SEQ], 1.0, LOWEST, ALU.add, ALU.max,
                                                           rowmax[half][:, n, c:c + 1])
                        ins.then_inc(s_mread[h], 1)
                    if group is not None and it.runs(offset):
                        divide(it, group, offset)
                    side(it, h)

            iterate(dve, step)

        @block.tensor
        def _(pe):
            pe.wait_ge(s_w, N_W)
            pe.wait_ge(s_lowc, 1)
            pe.matmul(bank6[:, 0:D], ones_row[:, :], bias_row[:, :], start=True, stop=True)
            pe.matmul(bank7[0:RANK, 0:D], down_s[:, :], daux_s[:, :], start=True, stop=True).then_inc(s_low, 1)
            pe.wait_ge(s_lowc, 2)
            pe.matmul(bank7[0:UDIM, 0:D], up_s[:, :], low1[:, :], start=True, stop=True).then_inc(s_low, 1)
            pe.wait_ge(s_lowc, 3)
            pe.matmul(bank7[:, 0:D], low2[:, :], uaux_s[:, :], start=True, stop=True).then_inc(s_low, 1)
            pe.wait_ge(s_lowc, 4)
            pe.wait_ge(s_const, N_CONST)
            pe.wait_ge(s_const2, 2)

            def max_scores(it, h):
                q, k = qx[it.ring(1)], kx[it.ring(1)]
                if h == 0:
                    pe.wait_ge(s_expand, it.done(1, EXPAND))
                pe.wait_ge(s_mread[(h - 2) % HEADS], it.done(1 if h >= 2 else 0))
                bank = max_bank[h % 2]
                pe.matmul(bank[:, 0:P], q[:, h, 0:P], k[:, h, 0:P], start=True, stop=True)
                pe.matmul(bank[:, P:PW], q[:, h, P:SEQ], k[:, h, 0:SEQ],
                          start=True, stop=True).then_inc(s_mscore[h], 1)

            def scores(it, h):
                q, k = qx[it.ring(0)], kx[it.ring(0)]
                if h % HALF == 0:
                    pe.wait_ge(s_mrow[h // HALF], it.done(0, MAX_ROWS))
                pe.wait_ge(s_exp[(h - 2) % HEADS], it.done(0 if h >= 2 else -1))
                bank = score_bank[h % 2]
                pe.matmul(bank[:, 0:SEQ], k[:, h, 0:P], q[:, h, :], start=True, stop=True)
                pe.matmul(bank[:, SEQ:PW], k[:, h, P:SEQ], q[:, h, P:SEQ],
                          start=True, stop=True).then_inc(s_score[h], 1)

            def pv(it, group, offset, n):
                r = it.ring(offset)
                if n == 0:
                    pe.wait_ge(s_mask[group], it.done(offset))
                    pe.wait_ge(s_norm[(group + 2) % GROUPS], it.done(offset if group >= 2 else offset - 1))
                    if group == 0:
                        pe.wait_ge(s_vx, it.done(offset))
                for g in range(GROUP):
                    h = GROUP * group + g
                    bank = pv_bank[group % 2][VW * g:VW * g + VW, :]
                    ins = pe.matmul(bank[:, n * P:SEQ], v_ext[r][:, n, h, :],
                                    probs[:, h, 0:SEQ] if n == 0 else probs[:, h, SEQ:PW],
                                    start=(n == 0), stop=(n == NB - 1), skip_group_check=True)
                if n == NB - 1:
                    ins.then_inc(s_pv[group], 1)

            def transpose2(bank, source, signal, at=0):
                for n in range(NB):
                    ins = pe.transpose(bank[:, at + n * P:at + n * P + P], source(n), ident[:, :])
                ins.then_inc(signal, 1)

            def pv_transpose(it, group, offset):
                pe.wait_ge(s_pvs[group], it.done(offset))
                transpose2(pv_bank[group % 2], lambda n: pv_s[group % 2][:, n * P:n * P + P], s_ot[group], at=SEQ)

            def max_transpose(it, half, offset, bank):
                pe.wait_ge(s_mp2[half], it.done(offset))
                for n in range(NB):
                    ins = pe.transpose(bank[:, :].bitcast(BF16)[0:MAX_PARTS * HALF, n * P:n * P + P],
                                       mpart[half][:, n, :, :].rearrange("p a h -> p (a h)"), ident_b[:, :])
                ins.then_inc(s_mTp[half], 1)

            def linear(bank, source, weight, signal):
                for n in range(NB):
                    ins = pe.matmul(bank[:, n * D:n * D + D], source[:, n * P:n * P + P], weight[:, :],
                                    start=True, stop=True)
                ins.then_inc(signal, 1)

            def in_bank6(it, h):
                if h == 0 and it.runs(2):
                    pe.wait_ge(s_yT, it.done(2))
                    pe.matmul(bank6[:, 0:SEQ], wq_s[:, :], yT[:, :], start=True, stop=True)
                    pe.matmul(bank6[:, SEQ:2 * SEQ], wk_s[:, :], yT[:, :], start=True, stop=True).then_inc(s_qk, 1)
                if h == 4 and it.runs(2):
                    pe.wait_ge(s_rest, it.done(2))
                    linear(bank6, yT, wv_s, s_v)
                if h == 8 and it.runs(-2):
                    pe.wait_ge(s_vx, it.done(2))
                    pe.wait_ge(s_mT[0], it.done(0))
                    pe.wait_ge(s_x1Ts, it.done(-3))
                    pe.wait_ge(s_x1, it.done(-2))
                    transpose2(bank6, lambda n: x1[:, n, :], s_x1T)
                if h == 10 and it.runs(1):
                    pe.wait_ge(s_vx, it.done(2))
                    pe.wait_ge(s_x1Ts, it.done(-2))
                    max_transpose(it, 0, 1, bank6)
                if h == 13 and it.runs(3):
                    pe.wait_ge(s_vx, it.done(2))
                    pe.wait_ge(s_x1Ts, it.done(-2))
                    pe.wait_ge(s_mT[0], it.done(1))
                    pe.wait_ge(s_xhat, it.done(3))
                    transpose2(bank6, lambda n: xhat[:, n, :], s_xT)

            def in_bank7(it, h):
                if h == 2 and it.runs(0):
                    pe.wait_ge(s_z, it.done(-2))
                    max_transpose(it, 1, 0, bank7)
                if h == 5 and it.runs(-3):
                    pe.wait_ge(s_mT[1], it.done(0))
                    pe.wait_ge(s_z, it.done(-2))
                    pe.wait_ge(s_f, it.done(-4))
                    pe.wait_ge(s_x1Ts, it.done(-3))
                    linear(bank7, x1T, wf_s, s_ff)
                if h == 10 and it.runs(-1):
                    pe.wait_ge(s_mT[1], it.done(0))
                    pe.wait_ge(s_z, it.done(-2))
                    pe.wait_ge(s_f, it.done(-3))
                    pe.wait_ge(s_norm[3], it.done(-1))
                    transpose2(bank7, lambda n: attn[:, n, :], s_aT)
                if h == 13 and it.runs(-1):
                    pe.wait_ge(s_aTs, it.done(-1))
                    linear(bank7, attnT, wo_s, s_wo)

            PVS = {3: (3, -1, 0), 4: (3, -1, 1), 7: (0, 0, 0), 8: (0, 0, 1), 11: (1, 0, 0), 12: (1, 0, 1),
                   15: (2, 0, 0), 0: (2, -1, 1)}

            PVTS = {7: (3, -1), 11: (0, 0), 15: (1, 0), 3: (2, -1)}

            def step(it):
                for h in range(HEADS):
                    if it.runs(1):
                        max_scores(it, h)
                    if it.runs(0):
                        scores(it, h)
                    if h in PVS:
                        group, offset, n = PVS[h]
                        if it.runs(offset):
                            pv(it, group, offset, n)
                    if h in PVTS:
                        group, offset = PVTS[h]
                        if it.runs(offset):
                            pv_transpose(it, group, offset)
                    in_bank6(it, h)
                    in_bank7(it, h)

            iterate(pe, step)


def kernel(**inputs):
    import numpy as np
    import concourse.bacc as bacc
    from concourse.bass_utils import run_bass_kernel_spmd

    def of(name):
        return np.asarray(inputs[name])

    def heads_inner(w):
        return w.transpose(1, 2, 0).reshape(D, D)

    arrays = {
        "x": of("L0_attn_x"),
        "ln_w": of("L0_attn_ln_w").reshape(D, 1),
        "ln_b": of("L0_attn_ln_b").reshape(D, 1),
        "wq": heads_inner(of("L0_attn_wq")),
        "wk": heads_inner(of("L0_attn_wk")),
        "wv": of("L0_attn_wv").transpose(1, 0, 2).reshape(D, D),
        "wo": of("L0_attn_wo"),
        "w_t": of("L0_ffn_W").T,
        "bias": of("L0_ffn_b").reshape(1, D),
        "down_t": of("L0_ffn_lora_down").T,
        "up_t": of("L0_ffn_lora_up").T,
        "down_aux": of("L0_ffn_down_aux"),
        "up_aux_t": of("L0_ffn_up_aux").T,
    }
    arrays = {f"in_{k}": np.ascontiguousarray(a) for k, a in arrays.items()}
    nc = bacc.Bacc("TRN2", target_bir_lowering=False, num_devices=1)
    args = [nc.dram_tensor(k, a.shape, mybir.dt.from_np(a.dtype), kind="ExternalInput").ap() for k, a in arrays.items()]
    out = nc.dram_tensor("out", (BATCHES, SEQ, D), F32, kind="ExternalOutput").ap()
    build(nc, *args, out)
    r = run_bass_kernel_spmd(nc, [arrays], core_ids=[0])
    return r.results[0]["out"]
```
